# Optimizing a Trainium2 kernel written in Bass

```python
import numpy as np
import jax
import jax.numpy as jnp

def _softmax(x, axis=-1):
    return jax.nn.softmax(x, axis=axis)

def _gelu(x):
    return jax.nn.gelu(x, approximate=True)

def _silu(x):
    return jax.nn.silu(x)

def _sigmoid(x):
    return jax.nn.sigmoid(x)

def _layernorm(x, axis=-1, eps=1e-05):
    m = jnp.mean(x, axis=axis, keepdims=True)
    v = jnp.var(x, axis=axis, keepdims=True)
    return (x - m) / jnp.sqrt(v + eps)

def _scatter_add(tgt, idx, src, axis=0):
    return tgt.at[idx].add(src)

def _segment_sum(src, seg, n):
    return jax.ops.segment_sum(src, seg, n)
kernel_name = 'mk_adaln_d2_jaxref_r8_0af8b9'

def setup_inputs(seed: int=0):
    np.random.seed(seed)
    _w = jnp.asarray

    def _L0_attn_setup():
        import jax, jax.numpy as jnp
        import numpy as np
        EMBED_DIM = 128
        NUM_HEADS = 16
        HEAD_DIM = EMBED_DIM // NUM_HEADS
        KERNEL_SIZE = 64
        B, L = (2, 256)
        key = jax.random.key(seed)
        ks = jax.random.split(key, 6)
        x = jax.random.normal(ks[0], (B, L, EMBED_DIM), dtype=jnp.float32)
        qkv_w = jax.random.normal(ks[1], (EMBED_DIM, 3 * EMBED_DIM), dtype=jnp.float32) / np.sqrt(EMBED_DIM)
        qkv_b = jnp.zeros((3 * EMBED_DIM,), dtype=jnp.float32)
        out_w = jax.random.normal(ks[2], (EMBED_DIM, EMBED_DIM), dtype=jnp.float32) / np.sqrt(EMBED_DIM)
        out_b = jnp.zeros((EMBED_DIM,), dtype=jnp.float32)
        proj = jax.random.normal(ks[3], (NUM_HEADS, HEAD_DIM, KERNEL_SIZE), dtype=jnp.float32) / np.sqrt(HEAD_DIM)
        return {'x': x, 'qkv_w': qkv_w, 'qkv_b': qkv_b, 'out_w': out_w, 'out_b': out_b, 'proj': proj}
    _L0_attn_in = _L0_attn_setup()

    def _L0_ffn_setup():
        import jax, jax.numpy as jnp
        import numpy as np
        B, L, D = (1, 256, 128)
        E, H, G, K = (64, 32, 64, 16)

        def _grouped_routing_scores(router_scores):
            T, En = router_scores.shape
            Tq = T // G
            budget = Tq * K
            order = jnp.argsort(-router_scores, axis=0)
            sorted_vals = jnp.take_along_axis(router_scores, order, axis=0)
            group_score = sorted_vals.reshape(Tq, G, En).sum(axis=1)
            _, top_flat = jax.lax.top_k(group_score.reshape(-1), budget)
            gmask = jnp.zeros((Tq * En,), bool).at[top_flat].set(True).reshape(Tq, En)
            mask_sorted = jnp.broadcast_to(gmask[:, None, :], (Tq, G, En)).reshape(T, En)
            mask = jnp.zeros((T, En), bool).at[order, jnp.arange(En)[None, :]].set(mask_sorted)
            fs = jnp.where(mask, router_scores, 0.0)
            return fs / (fs.sum(axis=-1, keepdims=True) + 1e-06)
        key = jax.random.key(seed)
        ks = jax.random.split(key, 6)
        s = lambda k, shape, scale: jax.random.normal(k, shape, jnp.float32) * scale
        return {'x': jax.random.normal(ks[0], (B, L, D), jnp.float32), 'Wr': s(ks[1], (D, E), D ** (-0.5)), 'br': jnp.zeros((E,), jnp.float32), 'Wup': s(ks[2], (E, D, H), D ** (-0.5)), 'bup': jnp.zeros((E, H), jnp.float32), 'Wgate': s(ks[3], (E, D, H), D ** (-0.5)), 'bgate': jnp.zeros((E, H), jnp.float32), 'Wdown': s(ks[4], (E, H, D), H ** (-0.5)), 'bdown': jnp.zeros((E, D), jnp.float32)}
    _L0_ffn_in = _L0_ffn_setup()
    _L0_c = _w((lambda *s: np.random.randn(*s).astype(np.float32) * 0.05)(4, 128))
    _L0_wmod = _w((lambda *s: np.random.randn(*s).astype(np.float32) * 0.05)(128, 6 * 128) * 128 ** (-0.5))

    def _L1_attn_setup():
        import jax, jax.numpy as jnp
        import numpy as np
        DIM = 128
        B, N = (8, 512)
        EPS = 1e-06
        key = jax.random.key(seed)
        k1, k2, k3, k4 = jax.random.split(key, 4)
        x = jax.random.normal(k1, (B, N, DIM), dtype=jnp.float32)
        s = 1.0 / np.sqrt(DIM)
        W_qkv = jax.random.uniform(k2, (3 * DIM, DIM), jnp.float32, -s, s)
        W_out = jax.random.uniform(k3, (DIM, DIM), jnp.float32, -s, s)
        b_out = jax.random.uniform(k4, (DIM,), jnp.float32, -s, s)
        return {'x': x, 'W_qkv': W_qkv, 'W_out': W_out, 'b_out': b_out}
    _L1_attn_in = _L1_attn_setup()

    def _L1_ffn_setup():
        import jax, jax.numpy as jnp
        import numpy as np
        BLOCK = 16
        _GRID = jnp.array([0.0, 0.5, 1.0, 1.5, 2.0, 3.0, 4.0, 6.0], dtype=jnp.float32)
        _MID = jnp.array([0.25, 0.75, 1.25, 1.75, 2.5, 3.5, 5.0], dtype=jnp.float32)

        def fp4_quant_dequant(x):
            shape = x.shape
            xb = x.reshape(shape[:-1] + (shape[-1] // BLOCK, BLOCK))
            scale = jnp.max(jnp.abs(xb), axis=-1, keepdims=True) / 6.0
            scale = jnp.maximum(scale, jnp.float32(1e-12))
            xn = xb / scale
            idx = jnp.searchsorted(_MID, jnp.abs(xn))
            q = _GRID[idx] * jnp.sign(xn) * scale
            return q.reshape(shape)

        def fp4_linear(x, w):
            xq = fp4_quant_dequant(x)
            wq = fp4_quant_dequant(w)
            return jnp.einsum('bsk,nk->bsn', xq, wq)
        key = jax.random.key(seed)
        k1, k2, k3, k4 = jax.random.split(key, 4)
        H, I = (128, 352)
        x = jax.random.normal(k1, (4, 512, H), dtype=jnp.float32)
        w_gate = jax.random.normal(k2, (I, H), dtype=jnp.float32) * 0.02
        w_up = jax.random.normal(k3, (I, H), dtype=jnp.float32) * 0.02
        w_down = jax.random.normal(k4, (H, I), dtype=jnp.float32) * 0.02
        return {'x': x, 'w_gate': w_gate, 'w_up': w_up, 'w_down': w_down}
    _L1_ffn_in = _L1_ffn_setup()
    _L1_c = _w((lambda *s: np.random.randn(*s).astype(np.float32) * 0.05)(4, 128))
    _L1_wmod = _w((lambda *s: np.random.randn(*s).astype(np.float32) * 0.05)(128, 6 * 128) * 128 ** (-0.5))
    _d = {'L0_attn_x': _L0_attn_in['x'], 'L0_attn_qkv_w': _L0_attn_in['qkv_w'], 'L0_attn_qkv_b': _L0_attn_in['qkv_b'], 'L0_attn_out_w': _L0_attn_in['out_w'], 'L0_attn_out_b': _L0_attn_in['out_b'], 'L0_attn_proj': _L0_attn_in['proj'], 'L0_ffn_Wr': _L0_ffn_in['Wr'], 'L0_ffn_br': _L0_ffn_in['br'], 'L0_ffn_Wup': _L0_ffn_in['Wup'], 'L0_ffn_bup': _L0_ffn_in['bup'], 'L0_ffn_Wgate': _L0_ffn_in['Wgate'], 'L0_ffn_bgate': _L0_ffn_in['bgate'], 'L0_ffn_Wdown': _L0_ffn_in['Wdown'], 'L0_ffn_bdown': _L0_ffn_in['bdown'], 'L0_c': _L0_c, 'L0_wmod': _L0_wmod, 'L1_attn_W_qkv': _L1_attn_in['W_qkv'], 'L1_attn_W_out': _L1_attn_in['W_out'], 'L1_attn_b_out': _L1_attn_in['b_out'], 'L1_ffn_w_gate': _L1_ffn_in['w_gate'], 'L1_ffn_w_up': _L1_ffn_in['w_up'], 'L1_ffn_w_down': _L1_ffn_in['w_down'], 'L1_c': _L1_c, 'L1_wmod': _L1_wmod}
    _x0 = _d['L0_attn_x']
    _d['L0_attn_x'] = jax.random.normal(jax.random.fold_in(jax.random.key(seed), 1), (4, 1024, 128), dtype=_x0.dtype)
    del _x0
    return _d

def reference(L0_attn_x, L0_attn_qkv_w, L0_attn_qkv_b, L0_attn_out_w, L0_attn_out_b, L0_attn_proj, L0_ffn_Wr, L0_ffn_br, L0_ffn_Wup, L0_ffn_bup, L0_ffn_Wgate, L0_ffn_bgate, L0_ffn_Wdown, L0_ffn_bdown, L0_c, L0_wmod, L1_attn_W_qkv, L1_attn_W_out, L1_attn_b_out, L1_ffn_w_gate, L1_ffn_w_up, L1_ffn_w_down, L1_c, L1_wmod):

    def _L0_attn_ref(x, qkv_w, qkv_b, out_w, out_b, proj):
        import jax, jax.numpy as jnp
        import numpy as np
        EMBED_DIM = 128
        NUM_HEADS = 16
        HEAD_DIM = EMBED_DIM // NUM_HEADS
        KERNEL_SIZE = 64
        B, L = (2, 256)
        Bn, Ln, E = x.shape
        H, D, M = proj.shape
        qkv = x @ qkv_w + qkv_b
        q, k, v = jnp.split(qkv, 3, axis=-1)
        q = q.reshape(Bn, Ln, H, D).transpose(0, 2, 1, 3)
        k = k.reshape(Bn, Ln, H, D).transpose(0, 2, 1, 3)
        v = v.reshape(Bn, Ln, H, D).transpose(0, 2, 1, 3)
        q_prime = jax.nn.relu(jnp.einsum('bhld,hdm->bhlm', q, proj))
        k_prime = jax.nn.relu(jnp.einsum('bhld,hdm->bhlm', k, proj))
        kv_prod = jnp.einsum('bhlm,bhld->bhlmd', k_prime, v)
        kv_cumsum = jnp.cumsum(kv_prod, axis=2)
        context = jnp.einsum('bhlm,bhlmd->bhld', q_prime, kv_cumsum)
        k_cumsum = jnp.cumsum(k_prime, axis=2)
        norm = jnp.einsum('bhlm,bhlm->bhl', q_prime, k_cumsum)
        out = context / (norm[..., None] + 1e-06)
        out = out.transpose(0, 2, 1, 3).reshape(Bn, Ln, E)
        return out @ out_w + out_b

    def _L0_ffn_ref(x, Wr, br, Wup, bup, Wgate, bgate, Wdown, bdown):
        import jax, jax.numpy as jnp
        import numpy as np
        B, L, D = (1, 256, 128)
        E, H, G, K = (64, 32, 64, 16)

        def _grouped_routing_scores(router_scores):
            T, En = router_scores.shape
            Tq = T // G
            budget = Tq * K
            order = jnp.argsort(-router_scores, axis=0)
            sorted_vals = jnp.take_along_axis(router_scores, order, axis=0)
            group_score = sorted_vals.reshape(Tq, G, En).sum(axis=1)
            _, top_flat = jax.lax.top_k(group_score.reshape(-1), budget)
            gmask = jnp.zeros((Tq * En,), bool).at[top_flat].set(True).reshape(Tq, En)
            mask_sorted = jnp.broadcast_to(gmask[:, None, :], (Tq, G, En)).reshape(T, En)
            mask = jnp.zeros((T, En), bool).at[order, jnp.arange(En)[None, :]].set(mask_sorted)
            fs = jnp.where(mask, router_scores, 0.0)
            return fs / (fs.sum(axis=-1, keepdims=True) + 1e-06)
        Bx, Lx, Dx = x.shape
        xt = x.reshape(-1, Dx)
        router_scores = jax.nn.softmax(xt @ Wr + br, axis=-1)
        fs = _grouped_routing_scores(router_scores)
        up = jnp.einsum('td,edh->teh', xt, Wup) + bup
        gate = jnp.einsum('td,edh->teh', xt, Wgate) + bgate
        h = jax.nn.silu(up) * gate * fs[:, :, None]
        out = jnp.einsum('teh,ehd->td', h, Wdown) + fs @ bdown
        return out.reshape(Bx, Lx, Dx)

    def _L1_attn_ref(x, W_qkv, W_out, b_out):
        import jax, jax.numpy as jnp
        import numpy as np
        DIM = 128
        B, N = (8, 512)
        EPS = 1e-06
        qkv = jnp.einsum('bnd,ed->bne', x, W_qkv)
        q, k, v = jnp.split(qkv, 3, axis=-1)
        q = jax.nn.relu(q) + EPS
        k = jax.nn.relu(k) + EPS
        kv = jnp.einsum('bnd,bne->bde', k, v)
        z = 1.0 / (jnp.einsum('bnd,bd->bn', q, k.sum(axis=1)) + EPS)
        attn = jnp.einsum('bnd,bde,bn->bne', q, kv, z)
        return jnp.einsum('bne,fe->bnf', attn, W_out) + b_out

    def _L1_ffn_ref(x, w_gate, w_up, w_down):
        import jax, jax.numpy as jnp
        import numpy as np
        BLOCK = 16
        _GRID = jnp.array([0.0, 0.5, 1.0, 1.5, 2.0, 3.0, 4.0, 6.0], dtype=jnp.float32)
        _MID = jnp.array([0.25, 0.75, 1.25, 1.75, 2.5, 3.5, 5.0], dtype=jnp.float32)

        def fp4_quant_dequant(x):
            shape = x.shape
            xb = x.reshape(shape[:-1] + (shape[-1] // BLOCK, BLOCK))
            scale = jnp.max(jnp.abs(xb), axis=-1, keepdims=True) / 6.0
            scale = jnp.maximum(scale, jnp.float32(1e-12))
            xn = xb / scale
            idx = jnp.searchsorted(_MID, jnp.abs(xn))
            q = _GRID[idx] * jnp.sign(xn) * scale
            return q.reshape(shape)

        def fp4_linear(x, w):
            xq = fp4_quant_dequant(x)
            wq = fp4_quant_dequant(w)
            return jnp.einsum('bsk,nk->bsn', xq, wq)
        gate = fp4_linear(x, w_gate)
        y = fp4_linear(x, w_up)
        h = jax.nn.silu(gate) * y
        return fp4_linear(h, w_down)
    x = L0_attn_x
    mod = (_silu(L0_c) @ L0_wmod).reshape(L0_c.shape[0], 6, 1, -1)
    sa, ca, ga, sb, cb, gb = (mod[:, 0], mod[:, 1], mod[:, 2], mod[:, 3], mod[:, 4], mod[:, 5])
    ga = (2 * (ga >= 0) - 1) * jnp.maximum(jnp.abs(ga), 0.25)
    gb = (2 * (gb >= 0) - 1) * jnp.maximum(jnp.abs(gb), 0.25)
    h = _layernorm(x, axis=-1) * (1 + ca) + sa
    x = x + ga * _L0_attn_ref(h, L0_attn_qkv_w, L0_attn_qkv_b, L0_attn_out_w, L0_attn_out_b, L0_attn_proj)
    h = _layernorm(x, axis=-1) * (1 + cb) + sb
    x = x + gb * _L0_ffn_ref(h, L0_ffn_Wr, L0_ffn_br, L0_ffn_Wup, L0_ffn_bup, L0_ffn_Wgate, L0_ffn_bgate, L0_ffn_Wdown, L0_ffn_bdown)
    mod = (_silu(L1_c) @ L1_wmod).reshape(L1_c.shape[0], 6, 1, -1)
    sa, ca, ga, sb, cb, gb = (mod[:, 0], mod[:, 1], mod[:, 2], mod[:, 3], mod[:, 4], mod[:, 5])
    ga = (2 * (ga >= 0) - 1) * jnp.maximum(jnp.abs(ga), 0.25)
    gb = (2 * (gb >= 0) - 1) * jnp.maximum(jnp.abs(gb), 0.25)
    h = _layernorm(x, axis=-1) * (1 + ca) + sa
    x = x + ga * _L1_attn_ref(h, L1_attn_W_qkv, L1_attn_W_out, L1_attn_b_out)
    h = _layernorm(x, axis=-1) * (1 + cb) + sb
    x = x + gb * _L1_ffn_ref(h, L1_ffn_w_gate, L1_ffn_w_up, L1_ffn_w_down)
    return x

_drawn_inputs = setup_inputs


def setup_inputs(seed=0):
    import zlib

    import numpy as np

    out = dict(_drawn_inputs(seed))
    spreads = {'L0_attn_qkv_b': (0.0, 0.274),
     'L0_attn_out_b': (0.0, 0.331),
     'L0_ffn_br': (0.0, 0.8),
     'L0_ffn_bup': (0.0, 0.8),
     'L0_ffn_bgate': (0.0, 0.8),
     'L0_ffn_bdown': (0.0, 0.8)}
    factors = {'L0_attn_proj': 6.927,
     'L1_attn_W_qkv': 8.0,
     'L1_attn_W_out': 8.0,
     'L1_attn_b_out': 4.544,
     'L1_ffn_w_gate': 8.0,
     'L1_ffn_w_up': 8.0,
     'L1_ffn_w_down': 8.0,
     'L1_c': 4.318,
     'L1_wmod': 4.304}
    for name, (base, spread) in spreads.items():
        noise = np.random.default_rng([zlib.crc32(name.encode()), seed]).standard_normal(out[name].shape)
        drawn = base * np.exp(spread * noise) if base else spread * noise
        out[name] = jnp.asarray(drawn.astype(out[name].dtype))
    for name, factor in factors.items():
        out[name] = (out[name] * factor).astype(out[name].dtype)
    return out
```

```python
from contextlib import ExitStack

import concourse.bass as bass
from concourse import mybir

F32 = mybir.dt.float32
F16 = mybir.dt.float16
BF16 = mybir.dt.bfloat16
U32 = mybir.dt.uint32
ALU = mybir.AluOpType
ACT = mybir.ActivationFunctionType
AX = mybir.AxisListType
ds = bass.ds

P = 128
NB = 4
L = 1024
T = NB * L
ST = 512
NC = L // P
WS = 64.0
NH, HD, MF = 16, 8, 64
E, HH = 64, 32
GS, NG = 64, T // 64
BUDGET = NG * 16
EBLK = E * HH // P
FS = 32768.0
LN_EPS = 1e-5
FIRST = 1
I_FF = 352
NBLK = [128, 128, 96]
QW = 6 * P + I_FF


class Chain:

    def __init__(self, eng, sem, turn=None, per=0, first=0):
        self.eng, self.sem, self.turn, self.per, self.n, self.first = eng, sem, turn, per, 0, first

    def __call__(self, ins):
        self.n += 1
        ins.then_inc(self.sem, 1)
        base = 0 if self.turn is None else self.turn * self.per
        self.eng.wait_ge(self.sem, base + self.first + self.n)

    def end(self):
        assert self.turn is None or self.n == self.per, self.n


def split_mm(nc, out, w_hi, w_lo, x_hi, x_lo, start=True, stop=True):
    nc.tensor.matmul(out, w_hi, x_hi, start=start, stop=False)
    nc.tensor.matmul(out, w_lo, x_hi, start=False, stop=False)
    return nc.tensor.matmul(out, w_hi, x_lo, start=False, stop=stop)


def fp4_quant(nc, step, src, dst, n, w):
    nb = n // 16
    blocks = lambda ap: ap.rearrange("p (b k) -> p b k", k=16)
    sc, rc = w["sc"][:, 0:nb], w["rc"][:, 0:nb]
    bc = lambda ap: ap.unsqueeze(2).to_broadcast([P, nb, 16])
    xn, ab, q, r = w["xn"][:, 0:n], w["ab"][:, 0:n], w["q"][:, 0:n], w["r"][:, 0:n]
    step(nc.vector.tensor_reduce(sc, blocks(src), AX.X, ALU.max, apply_absolute_value=True))
    step(nc.vector.tensor_scalar(sc, sc, 1.0 / 6.0, 1e-12, ALU.mult, ALU.max))
    step(nc.vector.reciprocal(rc, sc))
    step(nc.vector.tensor_tensor(blocks(xn), blocks(src), bc(rc), ALU.mult))
    step(nc.vector.tensor_scalar(ab.bitcast(U32), xn.bitcast(U32), 0x7FFFFFFF, None, ALU.bitwise_and))
    step(nc.vector.tensor_scalar(q, ab, 5.0, 2.0, ALU.is_gt, ALU.mult))
    step(nc.vector.scalar_tensor_tensor(q, ab, 3.5, q, ALU.is_gt, ALU.add))
    step(nc.vector.scalar_tensor_tensor(q, ab, 2.5, q, ALU.is_gt, ALU.add))
    step(nc.vector.tensor_scalar(r, ab, 1.75, None, ALU.is_gt))
    step(nc.vector.scalar_tensor_tensor(r, ab, 1.25, r, ALU.is_gt, ALU.add))
    step(nc.vector.scalar_tensor_tensor(r, ab, 0.75, r, ALU.is_gt, ALU.add))
    step(nc.vector.scalar_tensor_tensor(r, ab, 0.25, r, ALU.is_gt, ALU.add))
    step(nc.vector.scalar_tensor_tensor(q, r, 0.5, q, ALU.mult, ALU.add))
    step(nc.vector.scalar_tensor_tensor(q.bitcast(U32), xn.bitcast(U32), 0x80000000, q.bitcast(U32),
                                        ALU.bitwise_and, ALU.bitwise_or))
    return nc.vector.tensor_tensor(blocks(dst), blocks(q), bc(sc), ALU.mult)


FP4_STEPS = 14


def program(nc, x, qkv_w, qkv_b, out_w, out_b, proj, Wr, br, Wup, bup, Wgate, bgate, Wdown, bdown,
            c0, wmod0, W_qkv1, W_out1, b_out1, w_gate, w_up, w_down, c1, wmod1, out):
    x_t = x.rearrange("b (s p) d -> (b s) p d", p=P)
    out_t = out.rearrange("b (s p) d -> (b s) p d", p=P)
    ctx = ExitStack()
    with ctx:
        def sb(name, shape, dt=F32):
            return ctx.enter_context(nc.sbuf_tensor(name, shape, dt))

        def scoped(stage):
            taken = []

            def stand(dma=()):
                for h in taken:
                    nc.sync.sem_inc(h, 16 if h in dma else FIRST)
                nc.all_engine_barrier()

            def clear():
                nums = sorted(h.num for h in taken)
                runs = [n for n in nums if n - 1 not in nums]
                for first in runs:
                    last = next(n for n in nums if n >= first and n + 1 not in nums)
                    nc.gpsimd.sem_clear(range(first, last + 1))
                nc.all_engine_barrier()

            def sem(name):
                taken.append(stage.enter_context(nc.semaphore(name)))
                return taken[-1]

            stage.callback(clear)
            return sem, stand

        bank = [ctx.enter_context(nc.psum_tensor(f"bank{i}", [P, ST], F32)) for i in range(8)]

        XT = sb("XT", [P, T])
        Hhi, Hlo = sb("Hhi", [P, T], F16), sb("Hlo", [P, T], F16)
        ident = sb("ident", [P, P])
        mean_w = sb("mean_w", [P, P])
        eps_ln = sb("eps_ln", [P, 1])
        mod = sb("mod", [P, 2, 6, NB])
        ga_bo = sb("ga_bo", [P, 2, NB])
        Wf = [[sb(f"Wf{i}{j}", [P, NH * MF], F16) for j in "hl"] for i in "qk"]
        Wv = [sb(f"Wv{j}", [P, P], F16) for j in "hl"]
        bf = sb("bf", [P, 8, 2])
        bv = sb("bv", [P, P])
        Wo0 = sb("Wo0", [P, P])
        causal = sb("causal", [P, 4, P])
        Wrs = [sb(f"Wrs{j}", [P, E], F16) for j in "hl"]
        brb = sb("brb", [P, E])
        RS = sb("RS", [P, T // 2])
        F2 = sb("F2", [P, T], F16)
        Wu = [sb(f"Wu{j}", [P, E * HH], F16) for j in "hl"]
        Wg = [sb(f"Wg{j}", [P, E * HH], F16) for j in "hl"]
        Wd = sb("Wd", [P, EBLK, P])
        bu, bg = sb("bu", [P, EBLK]), sb("bg", [P, EBLK])
        bd = [sb(f"bd{j}", [P, P], F16) for j in "hl"]
        spread = sb("spread", [P, EBLK, P], F16)
        ones16 = sb("ones16", [P, P], F16)
        ones32 = sb("ones32", [P, P])
        W1 = [sb(f"W1{j}", [P, 3 * P], F16) for j in "hl"]
        Wo1 = sb("Wo1", [P, P])
        wgT, wuT = sb("wgT", [P, I_FF]), sb("wuT", [P, I_FF])
        wdT = sb("wdT", [P, 3, P])

        with ExitStack() as tmp:
            sem, _ = scoped(tmp)

            def tb(name, shape, dt=F32):
                return tmp.enter_context(nc.sbuf_tensor(name, shape, dt))

            w0 = tb("w0", [P, 3 * P])
            wqkT = tb("wqkT", [P, 2 * P])
            projbd = tb("projbd", [P, NH * MF])
            bqk = tb("bqk", [P, 2])
            cT = tb("cT", [P, 2, NB])
            wm = tb("wm", [P, 2, 6 * P])
            bo = tb("bo", [P, 2])
            sgn, mag = tb("sgn", [P, 2, NB]), tb("mag", [P, 2, NB])
            wr_f, bd_f = tb("wr_f", [P, E]), tb("bd_f", [P, P])
            wu_f, wg_f = tb("wu_f", [P, E * HH]), tb("wg_f", [P, E * HH])
            w1_f, wo1_f = tb("w1_f", [P, 3, P]), tb("wo1_f", [P, P])
            wq_n, wq_q = tb("wq_n", [P, QW]), tb("wq_q", [P, QW])
            work = {k: tb("prep_" + k, [P, QW]) for k in ("xn", "ab", "q", "r")}
            work |= {k: tb("prep_" + k, [P, QW // 16]) for k in ("sc", "rc")}
            xin = tb("xin", [P, 8, 4, P])

            s_zero = sem("prep_zero")
            s_const = sem("prep_const")
            s_load = sem("prep_load")
            s_ew = sem("prep_ew")
            s_l1 = sem("prep_l1")
            s_silu = sem("prep_silu")
            s_mod = sem("prep_mod")
            s_wqt, s_wqtd = sem("prep_wqt"), sem("prep_wqtd")
            s_wf, s_wfd = sem("prep_wf"), sem("prep_wfd")
            s_q4, s_tr, s_trd = sem("prep_q4"), sem("prep_tr"), sem("prep_trd")
            s_dve = sem("prep_dve")
            s_x = [sem(f"prep_x{i}") for i in range(8)]
            s_xt = [sem(f"prep_xt{i}") for i in range(2)]
            s_xtd = [sem(f"prep_xtd{i}") for i in range(2)]
            n_load = [0, 0, 0]
            N_CONST = 11
            with nc.allow_non_contiguous_dma("small transposed weights"), nc.Block() as block:
                @block.gpsimd
                def _(pool):
                    step = Chain(pool, s_const)
                    nc.gpsimd.memset(projbd[:], 0.0).then_inc(s_zero, 1)
                    nc.gpsimd.memset(wq_n[:], 0.0).then_inc(s_zero, 1)
                    pool.wait_ge(s_zero, 2)
                    step(nc.gpsimd.memset(ident[:], 1.0))
                    step(nc.gpsimd.affine_select(out=ident[:], in_=ident[:], compare_op=ALU.is_equal, fill=0.0,
                                                 base=0, pattern=[[-1, P]], channel_multiplier=1))
                    step(nc.gpsimd.memset(causal[:], 1.0))
                    step(nc.gpsimd.affine_select(out=causal[:], in_=causal[:], compare_op=ALU.is_ge, fill=0.0,
                                                 base=0, pattern=[[0, 4], [1, P]], channel_multiplier=-1))
                    step(nc.gpsimd.memset(mean_w[:], 1.0 / P))
                    step(nc.gpsimd.memset(eps_ln[:], LN_EPS))
                    step(nc.gpsimd.memset(ones16[:], 1.0))
                    step(nc.gpsimd.memset(ones32[:], 1.0))
                    step(nc.gpsimd.memset(spread[:], 1.0))
                    for part in range(2):
                        v = spread[E * part:E * part + E, :, :].rearrange("p k (a c) -> p k a c", c=HH)
                        step(nc.gpsimd.affine_select(out=v, in_=v, compare_op=ALU.is_equal, fill=0.0, base=0,
                                                     pattern=[[-4, EBLK], [-1, 4], [0, HH]], channel_multiplier=1))
                    assert step.n == N_CONST

                @block.sync
                def _(sp):
                    def load(which, s, dst, src):
                        sp.dma_start(dst, src).then_inc(s, 16)
                        n_load[which] += 16
                    load(0, s_load, w0[:], qkv_w[:, :])
                    for i in range(2):
                        load(0, s_load, bqk[:, i:i + 1], qkv_b[P * i:P * (i + 1)].unsqueeze(1))
                    load(0, s_load, bv[:], qkv_b[2 * P:3 * P].partition_broadcast(P))
                    for h in range(NH):
                        g, r = 2 * (h // 8) + h % 2, (h // 2) % 4
                        row = 32 * g + 8 * r
                        load(0, s_load, Wo0[row:row + HD, :], out_w[HD * h:HD * (h + 1), :])
                    load(0, s_load, bo[:, 0:1], out_b[:].unsqueeze(1))
                    load(0, s_load, bo[:, 1:2], b_out1[:].unsqueeze(1))
                    load(0, s_load, wm[:, 0, :], wmod0[:, :])
                    load(0, s_load, wm[:, 1, :], wmod1[:, :])
                    load(0, s_load, cT[:, 0, :], c0.rearrange("b k -> k b"))
                    load(0, s_load, cT[:, 1, :], c1.rearrange("b k -> k b"))
                    sp.wait_ge(s_zero, 2)
                    for h in range(NH):
                        load(0, s_load, projbd[HD * h:HD * (h + 1), MF * h:MF * (h + 1)], proj[h])
                    load(2, s_l1, w1_f[:], W_qkv1.rearrange("(a p) d -> p a d", p=P))
                    load(2, s_l1, wo1_f[:], W_out1[:, :])
                    for i, w in enumerate((w_gate, w_up)):
                        for k, n in enumerate(NBLK):
                            load(2, s_l1, wq_n[0:n, (3 * i + k) * P:(3 * i + k + 1) * P], w[P * k:P * k + n, :])
                    load(2, s_l1, wq_n[:, 6 * P:QW], w_down[:, :])
                    load(1, s_ew, wr_f[:], Wr[:, :])
                    load(1, s_ew, brb[:], br[:].partition_broadcast(P))
                    load(1, s_ew, wu_f[:].rearrange("p (e h) -> p e h", h=HH), Wup.rearrange("e d h -> d e h"))
                    load(1, s_ew, wg_f[:].rearrange("p (e h) -> p e h", h=HH), Wgate.rearrange("e d h -> d e h"))
                    load(1, s_ew, Wd[:], Wdown.rearrange("(k a) h d -> (a h) k d", a=4))
                    load(1, s_ew, bu[:], bup.rearrange("(k a) h -> (a h) k", a=4))
                    load(1, s_ew, bg[:], bgate.rearrange("(k a) h -> (a h) k", a=4))
                    for part in range(2):
                        load(1, s_ew, bd_f[E * part:E * part + E, :], bdown[:, :])

                @block.scalar
                def _(act):
                    for i in range(8):
                        act.dma_start(xin[:, i], x_t[4 * i:4 * i + 4].rearrange("s p d -> p s d")).then_inc(s_x[i], 16)
                    act.wait_ge(s_load, n_load[0])
                    nc.scalar.activation(cT[:], cT[:], ACT.Silu).then_inc(s_silu, 1)
                    for i in range(8):
                        act.wait_ge(s_xt[i % 2], i // 2 + 1)
                        nc.scalar.copy(XT[:, i * ST:(i + 1) * ST], bank[i % 2][:, :]).then_inc(s_xtd[i % 2], 1)

                @block.tensor
                def _(pe):
                    pe.wait_ge(s_const, 2)
                    for i in range(8):
                        pe.wait_ge(s_x[i], 16)
                        pe.wait_ge(s_xtd[i % 2], i // 2)
                        for c in range(4):
                            t = nc.tensor.transpose(bank[i % 2][:, c * P:(c + 1) * P], xin[:, i, c, :], ident[:])
                        t.then_inc(s_xt[i % 2], 1)
                    pe.wait_ge(s_silu, 1)
                    for l in range(2):
                        for j in range(6):
                            n = (l * 6 + j) * NB
                            m = nc.tensor.matmul(bank[2][:, n:n + NB], wm[:, l, j * P:(j + 1) * P], cT[:, l, :],
                                                 start=True, stop=True)
                    m.then_inc(s_mod, 1)
                    for i in range(2):
                        t = nc.tensor.transpose(bank[3][:, i * P:(i + 1) * P], w0[:, i * P:(i + 1) * P], ident[:])
                    t.then_inc(s_wqt, 1)
                    pe.wait_ge(s_wqtd, 1)
                    for i in range(2):
                        for k in range(2):
                            nc.tensor.matmul(bank[4 + 2 * i + k][:, :], wqkT[:, i * P:(i + 1) * P],
                                             projbd[:, k * ST:(k + 1) * ST], start=True, stop=True).then_inc(s_wf, 1)
                    for p in range(8):
                        m = nc.tensor.matmul(bank[3][:, 2 * p:2 * p + 2], projbd[:, p * P:(p + 1) * P], bqk[:, :],
                                             start=True, stop=True)
                    m.then_inc(s_wf, 1)
                    pe.wait_ge(s_l1, n_load[2])
                    pe.wait_ge(s_wfd, 1)
                    for i in range(3):
                        nc.tensor.transpose(bank[4][:, i * P:(i + 1) * P], w1_f[:, i, :], ident[:])
                    nc.tensor.transpose(bank[4][:, 3 * P:4 * P], wo1_f[:], ident[:]).then_inc(s_tr, 1)
                    pe.wait_ge(s_q4, 1)
                    for k, n in enumerate(NBLK):
                        for i in range(2):
                            nc.tensor.transpose(bank[5 + i][:, k * P:k * P + n],
                                                wq_q[0:n, (3 * i + k) * P:(3 * i + k + 1) * P], ident[0:n, 0:n])
                        t = nc.tensor.transpose(bank[7][0:n, k * P:(k + 1) * P],
                                                wq_q[:, 6 * P + k * P:6 * P + k * P + n], ident[:])
                    t.then_inc(s_tr, 1)

                @block.vector
                def _(dve):
                    step = Chain(dve, s_dve)
                    dve.wait_ge(s_mod, 1)
                    step(nc.vector.tensor_copy(mod[:].rearrange("p l j b -> p (l j b)"), bank[2][:, 0:12 * NB]))
                    for j in (1, 4):
                        step(nc.vector.tensor_scalar(mod[:, :, j, :], mod[:, :, j, :], 1.0, None, ALU.add))
                    for j in (2, 5):
                        step(nc.vector.tensor_scalar(sgn[:], mod[:, :, j, :], 0.0, 2.0, ALU.is_ge, ALU.mult))
                        step(nc.vector.scalar_tensor_tensor(mag[:], mod[:, :, j, :], -1.0, mod[:, :, j, :], ALU.mult, ALU.max))
                        step(nc.vector.tensor_scalar(mag[:], mag[:], 0.25, None, ALU.max))
                        step(nc.vector.scalar_tensor_tensor(mod[:, :, j, :], sgn[:], 1.0, mag[:], ALU.subtract, ALU.mult))
                    for l in range(2):
                        step(nc.vector.tensor_scalar(ga_bo[:, l, :], mod[:, l, 2, :], bo[:, l:l + 1], None, ALU.mult))
                    dve.wait_ge(s_wqt, 1)
                    nc.vector.tensor_copy(wqkT[:], bank[3][:, 0:2 * P]).then_inc(s_wqtd, 1)
                    dve.wait_ge(s_wf, 5)
                    for i in range(2):
                        for k in range(2):
                            hi, lo = (Wf[i][j][:, k * ST:(k + 1) * ST] for j in range(2))
                            step(nc.vector.tensor_scalar(hi, bank[4 + 2 * i + k][:, :], WS, None, ALU.mult))
                            step(nc.vector.scalar_tensor_tensor(lo, bank[4 + 2 * i + k][:, :], WS, hi, ALU.mult,
                                                                ALU.subtract))
                    nc.vector.tensor_scalar(bf[:].rearrange("p a b -> p (a b)"), bank[3][:, 0:16], WS, None,
                                            ALU.mult).then_inc(s_wfd, 1)

                    def split(hi, lo, src):
                        step(nc.vector.tensor_scalar(hi, src, WS, None, ALU.mult))
                        step(nc.vector.scalar_tensor_tensor(lo, src, WS, hi, ALU.mult, ALU.subtract))
                    split(Wv[0][:], Wv[1][:], w0[:, 2 * P:3 * P])
                    dve.wait_ge(s_l1, n_load[2])
                    fp4_quant(nc, step, wq_n[:], wq_q[:], QW, work).then_inc(s_q4, 1)
                    dve.wait_ge(s_tr, 1)
                    split(W1[0][:], W1[1][:], bank[4][:, 0:3 * P])
                    nc.vector.tensor_copy(Wo1[:], bank[4][:, 3 * P:4 * P])
                    dve.wait_ge(s_ew, n_load[1])
                    split(Wrs[0][:], Wrs[1][:], wr_f[:])
                    split(Wu[0][:], Wu[1][:], wu_f[:])
                    split(Wg[0][:], Wg[1][:], wg_f[:])
                    split(bd[0][:], bd[1][:], bd_f[:])
                    step(nc.vector.tensor_scalar(bg[:], bg[:], WS, None, ALU.mult))
                    dve.wait_ge(s_tr, 2)
                    nc.vector.tensor_copy(wgT[:], bank[5][:, 0:I_FF])
                    nc.vector.tensor_copy(wuT[:], bank[6][:, 0:I_FF])
                    for k, n in enumerate(NBLK):
                        nc.vector.tensor_copy(wdT[0:n, k, :], bank[7][0:n, k * P:(k + 1) * P])


        def layer_norm(tag, l, j0, h32=None):
            with ExitStack() as tmp:
                sem, stand = scoped(tmp)
                def tb(name, dt=F32):
                    return [tmp.enter_context(nc.sbuf_tensor(f"{tag}_{name}{j}", [P, ST], dt)) for j in range(2)]
                xc, sq, rs, xn, hf = tb("xc"), tb("sq"), tb("rs"), tb("xn"), tb("hf")
                mean, var = bank[0:2], bank[2:4]
                s_mean, s_xc, s_sq, s_var, s_rs, s_xn, s_h, s_lo = (
                    [sem(f"{tag}_{n}{j}") for j in range(2)]
                    for n in ("mean", "xc", "sq", "var", "rs", "xn", "h", "lo"))
                s_ln, s_hi = sem(f"{tag}_ln"), sem(f"{tag}_hi")
                cols = lambda b, j: ds(b * L + j * ST, ST)
                stand()
                with nc.Block() as block:
                    @block.tensor
                    def _(pe):
                        with pe.Fori(0, NB) as b:
                            for j in range(2):
                                pe.wait_ge(s_xc[j], FIRST + b)
                                nc.tensor.matmul(mean[j][:, :], mean_w[:], XT[:, cols(b, j)], start=True,
                                                 stop=True).then_inc(s_mean[j], 1)
                            for j in range(2):
                                pe.wait_ge(s_sq[j], FIRST + b + 1)
                                nc.tensor.matmul(var[j][:, :], mean_w[:], sq[j][:], start=True,
                                                 stop=True).then_inc(s_var[j], 1)

                    @block.scalar
                    def _(act):
                        with act.Fori(0, NB) as b:
                            for j in range(2):
                                act.wait_ge(s_xc[j], FIRST + b + 1)
                                nc.scalar.activation(sq[j][:], xc[j][:], ACT.Square).then_inc(s_sq[j], 1)
                            for j in range(2):
                                act.wait_ge(s_var[j], FIRST + b + 1)
                                nc.scalar.activation(rs[j][:], var[j][:, :], ACT.Ln, bias=eps_ln[:]).then_inc(s_ln, 1)
                            for j in range(2):
                                act.wait_ge(s_ln, FIRST + b * 2 + j + 1)
                                nc.scalar.activation(rs[j][:], rs[j][:], ACT.Exp, scale=-0.5).then_inc(s_rs[j], 1)
                            for j in range(2):
                                act.wait_ge(s_xn[j], FIRST + b + 1)
                                if h32 is None:
                                    act.wait_ge(s_lo[j], FIRST + b)
                                dst = hf[j][:] if h32 is None else h32[:, cols(b, j)]
                                act.nop(nofuse=True)
                                nc.scalar.activation(dst, xn[j][:], ACT.Identity, bias=mod[:, l, j0, ds(b, 1)],
                                                     scale=mod[:, l, j0 + 1, ds(b, 1)]).then_inc(s_h[j], 1)

                    @block.vector
                    def _(dve):
                        with dve.Fori(0, NB) as b:
                            for j in range(2):
                                dve.wait_ge(s_mean[j], FIRST + b + 1)
                                dve.wait_ge(s_xn[j], FIRST + b)
                                nc.vector.tensor_tensor(xc[j][:], XT[:, cols(b, j)], mean[j][:, :],
                                                        ALU.subtract).then_inc(s_xc[j], 1)
                            for j in range(2):
                                dve.wait_ge(s_rs[j], FIRST + b + 1)
                                nc.vector.tensor_tensor(xn[j][:], xc[j][:], rs[j][:], ALU.mult).then_inc(s_xn[j], 1)
                            if h32 is None:
                                for j in range(2):
                                    dve.wait_ge(s_h[j], FIRST + b + 1)
                                    nc.vector.tensor_copy(Hhi[:, cols(b, j)], hf[j][:]).then_inc(s_hi, 1)
                                    dve.wait_ge(s_hi, FIRST + b * 2 + j + 1)
                                    nc.vector.tensor_tensor(Hlo[:, cols(b, j)], hf[j][:], Hhi[:, cols(b, j)],
                                                            ALU.subtract).then_inc(s_lo[j], 1)

        def causal_attention():
            with ExitStack() as tmp:
                sem, stand = scoped(tmp)
                def tb(name, shape):
                    return tmp.enter_context(nc.sbuf_tensor("att_" + name, shape, F32))
                qblk = tb("qblk", [P, 8, 2, ST])
                kp = tb("kp", [P, 8, ST])
                v1 = tb("v1", [P, 2, 4, NH, 32])
                am = tb("am", [P, NH * P])
                kt = tb("kt", [P, NH * MF])
                Sa = tb("Sa", [P, 256])
                Ss = tb("Ss", [P, 256])
                ob = tb("ob", [P, ST])
                den, rd = tb("den", [P, NH]), tb("rd", [P, NH])
                ck = tb("ck", [P, P])
                cT = tb("cT", [P, ST])
                yt = tb("yt", [P, ST])
                psF, psT, psA, psO, psS, psM = bank[0:2], bank[2], bank[3:5], bank[5], bank[6], bank[7]
                names = ("preset", "f", "qa", "qd", "ka", "v", "vd", "kt", "ktd", "A", "S", "Sd", "St", "Sv",
                         "O", "Od", "To", "den", "rd", "o2", "C", "cd", "Y", "yd", "xu")
                s = {n: sem("att_" + n) for n in names}
                s_m = [sem(f"att_m{i}") for i in range(2)]

                stand()
                with nc.Block() as block:
                    @block.gpsimd
                    def _(pool):
                        step = Chain(pool, s["preset"], first=FIRST)
                        step(nc.gpsimd.memset(qblk[64:128, :, 0, :], 0.0))
                        step(nc.gpsimd.memset(qblk[0:64, :, 1, :], 0.0))
                        step(nc.gpsimd.memset(v1[:], 0.0))
                        step(nc.gpsimd.memset(v1[:, :, :, :, HD:HD + 1], 1.0))

                    @block.tensor
                    def _(pe):
                        pe.wait_ge(s["preset"], FIRST + 4)
                        with pe.Fori(0, NB) as b:
                            free = [(s["yd"], b * 2)]

                            def take_psM():
                                pe.wait_ge(free[0][0], FIRST + free[0][1])

                            def post(c):
                                take_psM()
                                pe.wait_ge(s["Od"], FIRST + b * 8 + c + 1)
                                for g in range(4):
                                    t = nc.tensor.transpose(psM[:, g * P:(g + 1) * P], ob[:, g * P:(g + 1) * P],
                                                            ident[:])
                                t.then_inc(s["To"], 1)

                            def post2(c):
                                pe.wait_ge(s["o2"], FIRST + b * 8 + c + 1)
                                nc.tensor.transpose(psM[:, 0:P], ck[:], ident[:]).then_inc(s["C"], 1)
                                free[0] = (s["cd"], b * 8 + c + 1)

                            def out_proj(sc):
                                take_psM()
                                nc.tensor.matmul(psM[:, :], Wo0[:], cT[:], start=True, stop=True).then_inc(s["Y"], 1)
                                free[0] = (s["yd"], b * 2 + sc + 1)

                            for c in range(NC):
                                sc, cc = c // 4, c % 4
                                own = slice(cc * P, cc * P + P)
                                if cc == 0:
                                    cols = ds(b * L + sc * ST, ST)
                                    for p in range(8):
                                        w = slice(p * P, p * P + P)
                                        n = b * 16 + sc * 8 + p
                                        pe.wait_ge(s["qa"], FIRST + n)
                                        pe.wait_ge(s["qd"], FIRST + n)
                                        split_mm(nc, psF[0][:, :], Wf[0][0][:, w], Wf[0][1][:, w], Hhi[:, cols],
                                                 Hlo[:, cols]).then_inc(s["f"], 1)
                                        pe.wait_ge(s["ka"], FIRST + n)
                                        split_mm(nc, psF[1][:, :], Wf[1][0][:, w], Wf[1][1][:, w], Hhi[:, cols],
                                                 Hlo[:, cols]).then_inc(s["f"], 1)
                                    take_psM()
                                    for k in range(4):
                                        tk = ds(b * L + sc * ST + k * P, P)
                                        m = split_mm(nc, psM[:, k * P:k * P + P], Hhi[:, tk], Hlo[:, tk],
                                                     Wv[0][:], Wv[1][:])
                                    m.then_inc(s["v"], 1)
                                    free[0] = (s["vd"], b * 8 + sc * 4 + 4)
                                    pe.wait_ge(s["qa"], FIRST + b * 16 + sc * 8 + 8)
                                    pe.wait_ge(s["qd"], FIRST + b * 16 + sc * 8 + 8)
                                    pe.wait_ge(s["ka"], FIRST + b * 16 + sc * 8 + 8)

                                def k_by_token(n):
                                    pe.wait_ge(s["ktd"], FIRST + b * 16 + c * 2 + n)
                                    for p in range(4):
                                        t = nc.tensor.transpose(psT[:, p * P:p * P + P], kp[:, 4 * n + p, own], ident[:])
                                    t.then_inc(s["kt"], 1)

                                def scores(f):
                                    use = b * 16 + c * 2 + f // 2
                                    pe.wait_ge(s_m[f % 2], FIRST + use)
                                    for i in range(2):
                                        m = nc.tensor.matmul(psA[f % 2][:, i * 256:(i + 1) * 256],
                                                             kp[:, 2 * f + i, own], qblk[:, 2 * f + i, :, own],
                                                             start=True, stop=True)
                                    m.then_inc(s["A"], 1)

                                k_by_token(0)
                                scores(0)
                                k_by_token(1)
                                for f in (1, 2, 3):
                                    scores(f)
                                if c > 0:
                                    post(c - 1)
                                if c < NC - 1:
                                    pe.wait_ge(s["ktd"], FIRST + b * 16 + c * 2 + 2)
                                    pe.wait_ge(s["vd"], FIRST + b * 8 + sc * 4 + 4)
                                    pe.wait_ge(s["Sv"], FIRST + b * 7 + c)
                                    for gg in range(2):
                                        for half in range(2):
                                            for r in range(4):
                                                h, g = 8 * gg + 2 * r + half, 2 * gg + half
                                                m = nc.tensor.matmul(
                                                    psS[32 * r:32 * r + 32, g * MF:(g + 1) * MF], v1[:, sc, cc, h, :],
                                                    kt[:, h * MF:(h + 1) * MF], start=g == 0, stop=True,
                                                    skip_group_check=True, tile_position=(0, 32 * r))
                                    m.then_inc(s["S"], 1)
                                if c > 0:
                                    post2(c - 1)
                                pe.wait_ge(s["vd"], FIRST + b * 8 + sc * 4 + 4)
                                pe.wait_ge(s["Od"], FIRST + b * 8 + c)
                                for i in range(2):
                                    pe.wait_ge(s_m[i], FIRST + b * 16 + c * 2 + 2)
                                if c > 0:
                                    pe.wait_ge(s["Sv"], FIRST + b * 7 + c)
                                for gg in range(2):
                                    for half in range(2):
                                        g = 2 * gg + half
                                        for r in range(4):
                                            h, at = 8 * gg + 2 * r + half, psO[32 * r:32 * r + 32, g * P:(g + 1) * P]
                                            m = nc.tensor.matmul(at, v1[:, sc, cc, h, :], am[:, h * P:(h + 1) * P],
                                                                 start=g == 0, stop=c == 0, skip_group_check=True,
                                                                 tile_position=(0, 32 * r))
                                        if c > 0:
                                            for r in range(4):
                                                at = psO[32 * r:32 * r + 32, g * P:(g + 1) * P]
                                                m = nc.tensor.matmul(
                                                    at, Ss[:, gg * P + 32 * r:gg * P + 32 * r + 32],
                                                    qblk[:, 4 * gg + r, half, own], start=False, stop=True,
                                                    skip_group_check=True, tile_position=(0, 32 * r))
                                m.then_inc(s["O"], 1)
                                if c < NC - 1:
                                    pe.wait_ge(s["Sd"], FIRST + b * 7 + c + 1)
                                    for gg in range(2):
                                        t = nc.tensor.transpose(psS[:, 256 + gg * P:256 + (gg + 1) * P],
                                                                Sa[:, gg * P:(gg + 1) * P], ident[:])
                                    t.then_inc(s["St"], 1)
                                if c == 4:
                                    out_proj(0)
                            post(NC - 1)
                            post2(NC - 1)
                            out_proj(1)

                    @block.scalar
                    def _(act):
                        with act.Fori(0, NB) as b:
                            def finish(c):
                                act.wait_ge(s["C"], FIRST + b * 8 + c + 1)
                                nc.scalar.copy(cT[:, (c % 4) * P:(c % 4 + 1) * P], psM[:, 0:P]).then_inc(s["cd"], 1)

                            def gated(sc):
                                act.wait_ge(s["Y"], FIRST + b * 2 + sc + 1)
                                act.wait_ge(s["xu"], FIRST + b * 2 + sc)
                                act.nop(nofuse=True)
                                nc.scalar.activation(yt[:], psM[:, :], ACT.Identity, bias=ga_bo[:, 0, ds(b, 1)],
                                                     scale=mod[:, 0, 2, ds(b, 1)]).then_inc(s["yd"], 1)

                            for c in range(NC):
                                sc = c // 4
                                if c % 4 == 0:
                                    for p in range(8):
                                        n = b * 32 + sc * 16 + 2 * p
                                        act.wait_ge(s["f"], FIRST + n + 1)
                                        nc.scalar.activation(qblk[0:64, p, 0, :], psF[0][0:64, :], ACT.Relu,
                                                             bias=bf[0:64, p, 0:1]).then_inc(s["qa"], 1)
                                        act.wait_ge(s["f"], FIRST + n + 2)
                                        nc.scalar.activation(kp[:, p, :], psF[1][:, :], ACT.Relu,
                                                             bias=bf[:, p, 1:2]).then_inc(s["ka"], 1)
                                for n in range(2):
                                    act.wait_ge(s["kt"], FIRST + b * 16 + c * 2 + n + 1)
                                    nc.scalar.copy(kt[:, n * ST:(n + 1) * ST], psT[:, :]).then_inc(s["ktd"], 1)
                                if c > 0:
                                    finish(c - 1)
                                act.wait_ge(s["O"], FIRST + b * 8 + c + 1)
                                nc.scalar.copy(ob[:], psO[:, :]).then_inc(s["Od"], 1)
                                if c == 4:
                                    gated(0)
                            finish(NC - 1)
                            gated(1)

                    @block.vector
                    def _(dve):
                        with dve.Fori(0, NB) as b:
                            def divide(c):
                                n = b * 8 + c
                                res = psM[:, :].rearrange("p (a c) -> p a c", c=32)
                                dve.wait_ge(s["To"], FIRST + n + 1)
                                nc.vector.tensor_scalar(den[:], res[:, :, HD], WS * WS * 1e-6, None,
                                                        ALU.add).then_inc(s["den"], 1)
                                dve.wait_ge(s["den"], FIRST + n + 1)
                                nc.vector.reciprocal(rd[:], den[:]).then_inc(s["rd"], 1)
                                dve.wait_ge(s["rd"], FIRST + n + 1)
                                nc.vector.tensor_tensor(ck[:].rearrange("p (a c) -> p a c", c=HD), res[:, :, 0:HD],
                                                        rd[:].unsqueeze(2).to_broadcast([P, NH, HD]),
                                                        ALU.mult).then_inc(s["o2"], 1)

                            def add_x(sc):
                                cols = ds(b * L + sc * ST, ST)
                                dve.wait_ge(s["yd"], FIRST + b * 2 + sc + 1)
                                nc.vector.tensor_tensor(XT[:, cols], XT[:, cols], yt[:], ALU.add).then_inc(s["xu"], 1)

                            for c in range(NC):
                                sc = c // 4
                                if c % 4 == 0:
                                    for p in range(8):
                                        dve.wait_ge(s["f"], FIRST + b * 32 + sc * 16 + 2 * p + 1)
                                        nc.vector.tensor_scalar(qblk[64:128, p, 1, :], psF[0][64:128, :],
                                                                bf[64:128, p, 0:1], 0.0, ALU.add,
                                                                ALU.max).then_inc(s["qd"], 1)
                                    dve.wait_ge(s["v"], FIRST + b * 2 + sc + 1)
                                    for k in range(4):
                                        nc.vector.scalar_tensor_tensor(
                                            v1[:, sc, k, :, 0:HD],
                                            psM[:, k * P:k * P + P].rearrange("p (h e) -> p h e", e=HD), 1.0 / WS,
                                            bv[:].rearrange("p (h e) -> p h e", e=HD), ALU.mult,
                                            ALU.add).then_inc(s["vd"], 1)
                                for f in range(4):
                                    dve.wait_ge(s["A"], FIRST + b * 32 + c * 4 + f + 1)
                                    nc.vector.tensor_tensor(am[:, f * ST:(f + 1) * ST], psA[f % 2][:, :],
                                                            causal[:].rearrange("p a l -> p (a l)"),
                                                            ALU.mult).then_inc(s_m[f % 2], 1)
                                if c > 0:
                                    divide(c - 1)
                                if c < NC - 1:
                                    n = b * 7 + c + 1
                                    dve.wait_ge(s["S"], FIRST + n)
                                    if c == 0:
                                        nc.vector.tensor_copy(Sa[:], psS[:, 0:256]).then_inc(s["Sd"], 1)
                                    else:
                                        nc.vector.tensor_tensor(Sa[:], Sa[:], psS[:, 0:256], ALU.add).then_inc(s["Sd"], 1)
                                    dve.wait_ge(s["St"], FIRST + n)
                                    nc.vector.tensor_copy(Ss[:], psS[:, 256:512]).then_inc(s["Sv"], 1)
                                if c == 4:
                                    add_x(0)
                            divide(NC - 1)
                            add_x(1)

        def router():
            with ExitStack() as tmp:
                sem, stand = scoped(tmp)
                def tb(name, shape):
                    return [tmp.enter_context(nc.sbuf_tensor(f"rt_{name}{j}", shape, F32)) for j in range(2)]
                lg, ex, pr = tb("lg", [P, 4, E]), tb("ex", [P, 4, E]), tb("pr", [P, 4, E])
                mx, sm, rc = tb("mx", [P, 4]), tb("sm", [P, 4]), tb("rc", [P, 4])
                s_r, s_lg, s_ex, s_pr, s_t, s_td = (
                    [sem(f"rt_{n}{j}") for j in range(2)] for n in ("r", "lg", "ex", "pr", "t", "td"))
                s_dve = sem("rt_dve")
                bc = lambda ap: ap.unsqueeze(2).to_broadcast([P, 4, E])
                stand()
                with nc.Block() as block:
                    @block.tensor
                    def _(pe):
                        with pe.Fori(0, NB) as b:
                            for j in range(2):
                                pe.wait_ge(s_lg[j], FIRST + b)
                                for k in range(4):
                                    tk = ds(b * L + j * ST + k * P, P)
                                    m = split_mm(nc, bank[j][:, k * E:(k + 1) * E], Hhi[:, tk], Hlo[:, tk],
                                                 Wrs[0][:], Wrs[1][:])
                                m.then_inc(s_r[j], 1)
                            for j in range(2):
                                pe.wait_ge(s_pr[j], FIRST + b + 1)
                                pe.wait_ge(s_td[j], FIRST + b)
                                for k in range(2):
                                    t = nc.tensor.transpose(bank[2 + j][:, k * P:(k + 1) * P],
                                                            pr[j][:, 2 * k:2 * k + 2, :].rearrange("p c e -> p (c e)"),
                                                            ident[:])
                                t.then_inc(s_t[j], 1)

                    @block.scalar
                    def _(act):
                        with act.Fori(0, NB) as b:
                            for j in range(2):
                                act.wait_ge(s_lg[j], FIRST + b + 1)
                                nc.scalar.activation(ex[j][:], lg[j][:], ACT.Exp).then_inc(s_ex[j], 1)

                    @block.vector
                    def _(dve):
                        with dve.Fori(0, NB) as b:
                            step = Chain(dve, s_dve, b, 8, FIRST)
                            for j in range(2):
                                dve.wait_ge(s_r[j], FIRST + b + 1)
                                step(nc.vector.scalar_tensor_tensor(
                                    lg[j][:], bank[j][:, 0:4 * E].rearrange("p (c e) -> p c e", e=E), 1.0 / WS,
                                    brb[:].unsqueeze(1).to_broadcast([P, 4, E]), ALU.mult, ALU.add))
                                step(nc.vector.tensor_reduce(mx[j][:], lg[j][:], AX.X, ALU.max))
                                nc.vector.tensor_tensor(lg[j][:], lg[j][:], bc(mx[j][:]),
                                                        ALU.subtract).then_inc(s_lg[j], 1)
                            for j in range(2):
                                dve.wait_ge(s_ex[j], FIRST + b + 1)
                                step(nc.vector.tensor_reduce(sm[j][:], ex[j][:], AX.X, ALU.add))
                                step(nc.vector.reciprocal(rc[j][:], sm[j][:]))
                                nc.vector.tensor_tensor(pr[j][:], ex[j][:], bc(rc[j][:]), ALU.mult).then_inc(s_pr[j], 1)
                            for j in range(2):
                                dve.wait_ge(s_t[j], FIRST + b + 1)
                                nc.vector.tensor_copy(RS[:, ds(b * 512 + j * 256, 256)],
                                                      bank[2 + j][:, 0:256]).then_inc(s_td[j], 1)
                            step.end()

        def route():
            W = T // 2
            with ExitStack() as tmp:
                sem, stand = scoped(tmp)
                def tb(name, shape, dt=F32):
                    return tmp.enter_context(nc.sbuf_tensor("so_" + name, shape, dt))
                key = [tb("key0", [P, W]), tb("key1", [P, W])]
                other = tb("other", [P, W])
                G, gmin = tb("G", [P, 32]), tb("gmin", [P, 32])
                kk, th = tb("kk", [P, 16]), tb("th", [P, 16])
                lo, stp, jn = tb("lo", [P, 1]), tb("stp", [P, 1]), tb("jn", [P, 1])
                cmp_, cnt = tb("cmp", [P, 16, 32], BF16), tb("cnt", [P, 16], F16)
                jk = tb("jk", [P, 16])
                gt, eq, sel = tb("gt", [P, 32], F16), tb("eq", [P, 32], F16), tb("sel", [P, 32], F16)
                K, h01, ne = tb("K", [P, 1]), tb("h01", [P, 1]), tb("ne", [P, 1])
                cum, pre, gm = tb("cum", [P, 32]), tb("pre", [P, 32]), tb("gm", [P, 32])
                zero32 = tb("zero32", [P, 32])
                vh, vo, v = tb("vh", [P, 1]), tb("vo", [P, 1]), tb("v", [P, 1])
                cg, cg16, need = tb("cg", [P, 1]), tb("cg16", [P, 1], F16), tb("need", [P, 1])
                ends, nd = tb("ends", [P, 16], F16), tb("nd", [P, 16])
                below = tb("below", [P, P], F16)
                same_half = tb("same_half", [P, P], F16)
                first_half = tb("first_half", [P, P], F16)
                same_e = tb("same_e", [P, P], F16)
                swap = tb("swap", [P, P], F16)
                fhi, flo = tb("fhi", [P, W], F16), tb("flo", [P, W], F16)
                s_pc, s_dve, s_top = sem("so_pc"), sem("so_dve"), sem("so_top")
                s_sw, s_cnt, s_tot, s_rnd = sem("so_sw"), sem("so_cnt"), sem("so_tot"), sem("so_rnd")
                s_sorted, s_eq, s_pe, s_sel, s_ne = (sem("so_" + n) for n in ("sorted", "eq", "pe", "sel", "ne"))
                s_vh, s_vo, s_cg, s_cgt, s_ends, s_ofs, s_f, s_f2 = (
                    sem("so_" + n) for n in ("vh", "vo", "cg", "cgt", "ends", "ofs", "f", "f2"))
                ROUNDS = 12
                N_MASKS = 24

                with nc.allow_low_precision("counts up to 2048, exact in float16"), nc.Block() as block:
                    @block.gpsimd
                    def _(pool):
                        step = Chain(pool, s_pc)
                        for m in (below, same_half, first_half, same_e, swap, zero32, lo):
                            step(nc.gpsimd.memset(m[:], 0.0))
                        step(nc.gpsimd.memset(stp[:], GS / 16.0))
                        step(nc.gpsimd.iota(kk[:], pattern=[[1, 16]], base=1, channel_multiplier=0,
                                            allow_small_or_imprecise_dtypes=True))
                        a, z = slice(0, E), slice(E, P)
                        step(nc.gpsimd.memset(first_half[a, z], 1.0))
                        for h, o in ((a, z), (z, a)):
                            step(nc.gpsimd.memset(same_half[h, h], 1.0))
                            step(nc.gpsimd.memset(below[h, h], 1.0))
                            step(nc.gpsimd.affine_select(out=below[h, h], in_=below[h, h], compare_op=ALU.is_gt,
                                                         fill=0.0, base=0, pattern=[[1, E]], channel_multiplier=-1))
                            step(nc.gpsimd.memset(swap[h, o], 1.0))
                            step(nc.gpsimd.affine_select(out=swap[h, o], in_=swap[h, o], compare_op=ALU.is_equal,
                                                         fill=0.0, base=0, pattern=[[-1, E]], channel_multiplier=1))
                            step(nc.gpsimd.memset(same_e[h, :], 1.0))
                            step(nc.gpsimd.affine_select(out=same_e[h, :], in_=same_e[h, :], compare_op=ALU.is_equal,
                                                         fill=0.0, base=0, pattern=[[0, 2], [-1, E]],
                                                         channel_multiplier=1))
                        assert step.n == N_MASKS

                    @block.sync
                    def _(sp):
                        sp.wait_ge(s_top, 1)
                        sp.dma_start(other[0:E, :], key[0][E:P, :]).then_inc(s_sw, 16)
                        sp.dma_start(other[E:P, :], key[0][0:E, :]).then_inc(s_sw, 16)
                        sp.wait_ge(s_vh, 1)
                        sp.dma_start(vo[0:E, :], vh[E:P, :]).then_inc(s_vo, 16)
                        sp.dma_start(vo[E:P, :], vh[0:E, :]).then_inc(s_vo, 16)
                        for part, src in ((0, fhi), (1, flo)):
                            sp.wait_ge(s_f, part + 1)
                            for half in range(2):
                                dst = F2[E * part:E * part + E, :].rearrange("p (c a t) -> p c a t", a=2, t=P)
                                sp.dma_start(dst[:, :, half, :], src[E * half:E * half + E, :].rearrange(
                                    "p (c t) -> p c t", t=P)).then_inc(s_f2, 16)
                        sp.wait_ge(s_f2, 64)

                    @block.tensor
                    def _(pe):
                        pe.wait_ge(s_pc, N_MASKS)
                        with pe.Fori(0, ROUNDS) as r:
                            pe.wait_ge(s_cnt, r + 1)
                            nc.tensor.matmul(bank[0][:, 0:16], ones16[:], cnt[:], start=True, stop=True).then_inc(s_tot, 1)
                        pe.wait_ge(s_eq, 1)
                        nc.tensor.matmul(bank[1][:, 0:32], ones16[:], gt[:], start=True, stop=True)
                        nc.tensor.matmul(bank[1][:, 32:64], below[:], eq[:], start=True, stop=True)
                        nc.tensor.matmul(bank[1][:, 64:96], same_half[:], eq[:], start=True, stop=True)
                        nc.tensor.matmul(bank[1][:, 96:128], first_half[:], eq[:], start=True, stop=True).then_inc(s_pe, 1)
                        pe.wait_ge(s_sel, 1)
                        nc.tensor.matmul(bank[2][:, 0:32], same_e[:], sel[:], start=True, stop=True).then_inc(s_ne, 1)
                        pe.wait_ge(s_cg, 1)
                        nc.tensor.matmul(bank[3][:, 0:1], same_e[:], cg16[:], start=True, stop=True).then_inc(s_cgt, 1)
                        pe.wait_ge(s_ends, 1)
                        nc.tensor.matmul(bank[4][:, 0:16], swap[:], ends[:], start=True, stop=True).then_inc(s_ofs, 1)

                    @block.vector
                    def _(dve):
                        step = Chain(dve, s_dve)
                        cur, at = RS, 1

                        def exchange(size, flip):
                            nonlocal cur, at
                            at = 1 - at
                            a = cur[:].rearrange("p (n k) -> p n k", k=size)
                            o = key[at][:].rearrange("p (n k) -> p n k", k=size)
                            m = size // 2
                            first, second = a[:, :, 0:m], a[:, :, m:size]
                            if flip:
                                second = second[:, :, ::-1]
                            nc.vector.tensor_tensor(o[:, :, 0:m], first, second, ALU.max)
                            step(nc.vector.tensor_tensor(o[:, :, m:size], first, second, ALU.min))
                            cur = key[at]

                        size = 2
                        while size <= W:
                            exchange(size, True)
                            m = size // 2
                            while m > 1:
                                exchange(m, False)
                                m //= 2
                            size *= 2
                        if cur is not key[0]:
                            step(nc.vector.tensor_copy(key[0][:], cur[:]))
                        nc.vector.drain().then_inc(s_top, 1)
                        dve.wait_ge(s_sw, 32)
                        nc.vector.tensor_tensor(key[1][0:E, :], key[0][0:E, :], other[0:E, ::-1], ALU.max)
                        step(nc.vector.tensor_tensor(key[1][E:P, :], key[0][E:P, :], other[E:P, ::-1], ALU.min))
                        cur, at = key[1], 1
                        m = W
                        while m > GS:
                            exchange(m, False)
                            m //= 2
                        groups = cur[:].rearrange("p (g k) -> p g k", k=GS)
                        step(nc.vector.tensor_reduce(G[:], groups, AX.X, ALU.add))
                        step(nc.vector.tensor_reduce(gmin[:], groups, AX.X, ALU.min))
                        dve.wait_ge(s_pc, N_MASKS)

                        with dve.Fori(0, ROUNDS) as r:
                            rs = Chain(dve, s_rnd, r, 5)
                            rs(nc.vector.tensor_scalar(th[:], kk[:], stp[:], lo[:], ALU.mult, ALU.add))
                            rs(nc.vector.tensor_tensor(cmp_[:], G[:].unsqueeze(1).to_broadcast([P, 16, 32]),
                                                       th[:].unsqueeze(2).to_broadcast([P, 16, 32]), ALU.is_ge))
                            nc.vector.tensor_reduce(cnt[:], cmp_[:], AX.X, ALU.add).then_inc(s_cnt, 1)
                            dve.wait_ge(s_tot, r + 1)
                            rs(nc.vector.tensor_scalar(jk[:], bank[0][:, 0:16], float(BUDGET), None, ALU.is_ge, ALU.add,
                                                       accum_out=jn[:]))
                            rs(nc.vector.scalar_tensor_tensor(lo[:], jn[:], stp[:], lo[:], ALU.mult, ALU.add))
                            rs(nc.vector.tensor_scalar(stp[:], stp[:], 1.0 / 16.0, None, ALU.mult))
                            rs.end()
                        step(nc.vector.tensor_scalar(gt[:], G[:], lo[:], None, ALU.is_gt))
                        nc.vector.tensor_scalar(eq[:], G[:], lo[:], None, ALU.is_equal).then_inc(s_eq, 1)
                        dve.wait_ge(s_eq, 1)
                        dve.wait_ge(s_pe, 1)
                        step(nc.vector.tensor_reduce(K[:], bank[1][:, 0:32], AX.X, ALU.add))
                        step(nc.vector.tensor_scalar(K[:], K[:], -1.0, float(BUDGET), ALU.mult, ALU.add))
                        step(nc.vector.tensor_reduce(h01[:], bank[1][:, 96:128], AX.X, ALU.add))
                        step(nc.vector.tensor_tensor_scan(cum[:], bank[1][:, 64:96], zero32[:], 0.0, ALU.add, ALU.add))
                        step(nc.vector.tensor_tensor(cum[:], cum[:], bank[1][:, 64:96], ALU.subtract))
                        step(nc.vector.scalar_tensor_tensor(pre[:], bank[1][:, 32:64], h01[:], cum[:], ALU.add, ALU.add))
                        step(nc.vector.scalar_tensor_tensor(pre[:], pre[:], K[:], eq[:], ALU.is_lt, ALU.mult))
                        nc.vector.tensor_tensor(sel[:], pre[:], gt[:], ALU.add).then_inc(s_sel, 1)
                        dve.wait_ge(s_sel, 1)
                        step(nc.vector.tensor_scalar(gm[:], sel[:], -2.0, 2.0, ALU.mult, ALU.add))
                        step(nc.vector.tensor_tensor(gm[:], gm[:], gmin[:], ALU.max))
                        nc.vector.tensor_reduce(vh[:], gm[:], AX.X, ALU.min).then_inc(s_vh, 1)
                        dve.wait_ge(s_ne, 1)
                        step(nc.vector.tensor_reduce(ne[:], bank[2][:, 0:32], AX.X, ALU.add))
                        dve.wait_ge(s_vh, 1)
                        dve.wait_ge(s_vo, 32)
                        step(nc.vector.tensor_tensor(v[:], vh[:], vo[:], ALU.min))
                        step(nc.vector.tensor_scalar(key[0][:], RS[:], v[:], None, ALU.is_gt, ALU.add, accum_out=cg[:]))
                        nc.vector.tensor_copy(cg16[:], cg[:]).then_inc(s_cg, 1)
                        step(nc.vector.tensor_scalar(key[1][:], RS[:], v[:], None, ALU.is_equal))
                        dve.wait_ge(s_cgt, 1)
                        step(nc.vector.scalar_tensor_tensor(need[:], ne[:], float(GS), bank[3][:, 0:1], ALU.mult,
                                                            ALU.subtract))
                        step(nc.vector.tensor_tensor_scan(other[:], key[1][:], key[1][:], 0.0, ALU.add, ALU.max))
                        run = other[:].rearrange("p (c t) -> p c t", t=P)
                        nc.vector.tensor_copy(ends[:], run[:, :, P - 1]).then_inc(s_ends, 1)
                        dve.wait_ge(s_ofs, 1)
                        step(nc.vector.tensor_copy(nd[E:P, :], bank[4][E:P, 0:16]))
                        step(nc.vector.tensor_copy(nd[0:E, 1:16], bank[4][0:E, 0:15]))
                        step(nc.vector.memset(nd[0:E, 0:1], 0.0))
                        step(nc.vector.tensor_scalar(nd[:], nd[:], -1.0, need[:], ALU.mult, ALU.add))
                        step(nc.vector.tensor_tensor(run, run, nd[:].unsqueeze(2).to_broadcast([P, 16, P]), ALU.is_le))
                        step(nc.vector.tensor_tensor(other[:], other[:], key[1][:], ALU.mult))
                        step(nc.vector.tensor_tensor(other[:], other[:], key[0][:], ALU.add))
                        step(nc.vector.tensor_tensor(other[:], other[:], RS[:], ALU.mult))
                        nc.vector.tensor_scalar(fhi[:], other[:], FS, None, ALU.mult).then_inc(s_f, 1)
                        dve.wait_ge(s_f, 1)
                        nc.vector.scalar_tensor_tensor(flo[:], other[:], FS, fhi[:], ALU.mult,
                                                       ALU.subtract).then_inc(s_f, 1)

        def experts():
            with ExitStack() as tmp:
                sem, stand = scoped(tmp)
                def tb(name):
                    return [tmp.enter_context(nc.sbuf_tensor(f"ex_{name}{j}", [P, ST], F32)) for j in range(2)]
                u, pg, hh = tb("u"), tb("pg"), tb("hh")
                rec, y = tb("rec"), tb("y")
                psU, psG, psW, psY, psD = bank[0:2], bank[2:4], bank[4:6], bank[6], bank[7]
                s_U, s_in, s_u, s_g, s_hh, s_dn = (
                    [sem(f"ex_{n}{j}") for j in range(2)] for n in ("U", "in", "u", "g", "hh", "dn"))
                s_D, s_dd, s_rec, s_Y, s_y, s_x = (sem("ex_" + n) for n in ("D", "dd", "rec", "Y", "y", "x"))
                stand()
                with nc.Block() as block:
                    @block.tensor
                    def _(pe):
                        with pe.Fori(0, NB) as b:
                            for j in range(2):
                                cols = ds(b * L + j * ST, ST)
                                for k in range(EBLK + 1):
                                    if k < EBLK:
                                        q, use = k % 2, b * EBLK + j * (EBLK // 2) + k // 2
                                        w = slice(k * P, k * P + P)
                                        pe.wait_ge(s_u[q], FIRST + use)
                                        split_mm(nc, psU[q][:, :], Wu[0][:, w], Wu[1][:, w], Hhi[:, cols],
                                                 Hlo[:, cols]).then_inc(s_U[q], 1)
                                        pe.wait_ge(s_g[q], FIRST + use)
                                        split_mm(nc, psG[q][:, :], Wg[0][:, w], Wg[1][:, w], Hhi[:, cols],
                                                 Hlo[:, cols])
                                        pe.wait_ge(s_hh[q], FIRST + use)
                                        nc.tensor.matmul(psW[q][:, :], spread[:, k, :], F2[:, cols], start=True,
                                                         stop=True).then_inc(s_in[q], 1)
                                    if k == 0:
                                        pe.wait_ge(s_dd, FIRST + b * 2 + j)
                                        nc.tensor.matmul(psD[:, :], ones16[:], F2[:, cols], start=True,
                                                         stop=True).then_inc(s_D, 1)
                                        pe.wait_ge(s_y, FIRST + b * 2 + j)
                                        for i in range(2):
                                            nc.tensor.matmul(psY[:, :], bd[i][:], F2[:, cols], start=i == 0,
                                                             stop=False)
                                    else:
                                        q, use = (k - 1) % 2, b * EBLK + j * (EBLK // 2) + (k - 1) // 2
                                        pe.wait_ge(s_hh[q], FIRST + use + 1)
                                        m = nc.tensor.matmul(psY[:, :], Wd[:, k - 1, :], hh[q][:], start=False,
                                                             stop=k == EBLK)
                                        m.then_inc(s_dn[q], 1)

                    @block.scalar
                    def _(act):
                        with act.Fori(0, NB) as b:
                            for j in range(2):
                                for k in range(EBLK):
                                    q, use = k % 2, b * EBLK + j * (EBLK // 2) + k // 2
                                    act.wait_ge(s_U[q], FIRST + use + 1)
                                    act.wait_ge(s_g[q], FIRST + use)
                                    nc.scalar.activation(u[q][:], psU[q][:, :], ACT.Silu, bias=bu[:, k:k + 1],
                                                         scale=1.0 / WS).then_inc(s_u[q], 1)

                    @block.vector
                    def _(dve):
                        with dve.Fori(0, NB) as b:
                            for j in range(2):
                                n = b * 2 + j
                                cols = ds(b * L + j * ST, ST)
                                for k in range(EBLK):
                                    q, use = k % 2, b * EBLK + j * (EBLK // 2) + k // 2
                                    dve.wait_ge(s_in[q], FIRST + use + 1)
                                    dve.wait_ge(s_u[q], FIRST + use + 1)
                                    nc.vector.scalar_tensor_tensor(pg[q][:], psG[q][:, :], bg[:, k:k + 1], u[q][:],
                                                                   ALU.add, ALU.mult).then_inc(s_g[q], 1)
                                    dve.wait_ge(s_g[q], FIRST + use + 1)
                                    dve.wait_ge(s_dn[q], FIRST + use)
                                    nc.vector.tensor_tensor(hh[q][:], pg[q][:], psW[q][:, :],
                                                            ALU.mult).then_inc(s_hh[q], 1)
                                    if k == 1:
                                        dve.wait_ge(s_D, FIRST + n + 1)
                                        nc.vector.tensor_scalar(rec[0][:], psD[:, :], FS * 1e-6, WS, ALU.add,
                                                                ALU.mult).then_inc(s_dd, 1)
                                        dve.wait_ge(s_dd, FIRST + n + 1)
                                        nc.vector.reciprocal(rec[1][:], rec[0][:]).then_inc(s_rec, 1)
                                dve.wait_ge(s_rec, FIRST + n + 1)
                                dve.wait_ge(s_dn[1], FIRST + b * EBLK + (j + 1) * (EBLK // 2))
                                nc.vector.tensor_tensor(y[0][:], psY[:, :], rec[1][:], ALU.mult).then_inc(s_y, 1)
                                dve.wait_ge(s_y, FIRST + n + 1)
                                nc.vector.scalar_tensor_tensor(XT[:, cols], y[0][:], mod[:, 0, 5, ds(b, 1)],
                                                               XT[:, cols], ALU.mult, ALU.add).then_inc(s_x, 1)

        def linear_attention():
            EPS = 1e-6
            with ExitStack() as tmp:
                sem, stand = scoped(tmp)
                def tb(name, shape):
                    return tmp.enter_context(nc.sbuf_tensor("la_" + name, shape, F32))
                qT = tb("qT", [P, L])
                kt = [tb(f"kt{i}", [P, P]) for i in range(2)]
                vt = [tb(f"vt{i}", [P, P + 1]) for i in range(2)]
                kv, ksb = tb("kv", [P, P]), tb("ksb", [P, P])
                dn, rc = tb("dn", [P, ST]), tb("rc", [P, ST])
                at = [tb(f"at{i}", [P, ST]) for i in range(2)]
                ot = [tb(f"ot{i}", [P, ST]) for i in range(2)]
                psQ, psKV, psA, psN, psD, psO = bank[0:2], bank[2:4], bank[4], bank[5], bank[6], bank[7]
                s_q, s_qd, s_kv, s_k, s_v, s_acc, s_xu = (
                    [sem(f"la_{n}{j}") for j in range(2)] for n in ("q", "qd", "kv", "k", "v", "acc", "xu"))
                s_one, s_kvd, s_nd, s_dn, s_at, s_o, s_ot = (
                    sem("la_" + n) for n in ("one", "kvd", "nd", "dn", "at", "o", "ot"))
                stand()
                with nc.Block() as block:
                    @block.gpsimd
                    def _(pool):
                        for i in range(2):
                            nc.gpsimd.memset(vt[i][:, P:P + 1], 1.0).then_inc(s_one, 1)

                    @block.tensor
                    def _(pe):
                        pe.wait_ge(s_one, FIRST + 2)
                        with pe.Fori(0, NB) as b:
                            for j in range(2):
                                cols = ds(b * L + j * ST, ST)
                                pe.wait_ge(s_qd[j], FIRST + b)
                                split_mm(nc, psQ[j][:, :], W1[0][:, 0:P], W1[1][:, 0:P], Hhi[:, cols],
                                         Hlo[:, cols]).then_inc(s_q[j], 1)
                            for c in range(NC + 1):
                                if c < NC:
                                    i, use = c % 2, b * 4 + c // 2
                                    tk = ds(b * L + c * P, P)
                                    pe.wait_ge(s_k[i], FIRST + use)
                                    pe.wait_ge(s_v[i], FIRST + use)
                                    split_mm(nc, psKV[i][:, 0:2 * P], Hhi[:, tk], Hlo[:, tk], W1[0][:, P:3 * P],
                                             W1[1][:, P:3 * P]).then_inc(s_kv[i], 1)
                                if c == 1:
                                    pe.wait_ge(s_kvd, FIRST + b * 2)
                                if c > 0:
                                    i, use = (c - 1) % 2, b * 4 + (c - 1) // 2
                                    pe.wait_ge(s_k[i], FIRST + use + 1)
                                    pe.wait_ge(s_v[i], FIRST + use + 1)
                                    nc.tensor.matmul(psA[:, 0:P + 1], kt[i][:], vt[i][:], start=c == 1,
                                                     stop=c == NC).then_inc(s_acc[i], 1)
                            pe.wait_ge(s_kvd, FIRST + b * 2 + 2)
                            for j in range(2):
                                pe.wait_ge(s_qd[j], FIRST + b + 1)
                            for j in range(2):
                                own = slice(j * ST, (j + 1) * ST)
                                pe.wait_ge(s_at, FIRST + b * 2 + j)
                                nc.tensor.matmul(psN[:, :], kv[:], qT[:, own], start=True, stop=True)
                                nc.tensor.matmul(psD[:, :], ksb[:], qT[:, own], start=True, stop=True).then_inc(s_nd, 1)
                                pe.wait_ge(s_at, FIRST + b * 2 + j + 1)
                                pe.wait_ge(s_ot, FIRST + b * 2 + j)
                                nc.tensor.matmul(psO[:, :], Wo1[:], at[j][:], start=True, stop=True).then_inc(s_o, 1)

                    @block.scalar
                    def _(act):
                        with act.Fori(0, NB) as b:
                            for c in range(NC):
                                i, use = c % 2, b * 4 + c // 2
                                act.wait_ge(s_kv[i], FIRST + use + 1)
                                act.wait_ge(s_acc[i], FIRST + use)
                                nc.scalar.copy(vt[i][:, 0:P], psKV[i][:, P:2 * P]).then_inc(s_v[i], 1)
                            for j in range(2):
                                act.wait_ge(s_o, FIRST + b * 2 + j + 1)
                                act.wait_ge(s_xu[j], FIRST + b)
                                act.nop(nofuse=True)
                                nc.scalar.activation(ot[j][:], psO[:, :], ACT.Identity, bias=ga_bo[:, 1, ds(b, 1)],
                                                     scale=mod[:, 1, 2, ds(b, 1)]).then_inc(s_ot, 1)

                    @block.vector
                    def _(dve):
                        with dve.Fori(0, NB) as b:
                            for j in range(2):
                                dve.wait_ge(s_q[j], FIRST + b + 1)
                                nc.vector.tensor_scalar(qT[:, j * ST:(j + 1) * ST], psQ[j][:, :], 0.0, WS * EPS,
                                                        ALU.max, ALU.add).then_inc(s_qd[j], 1)
                            for c in range(NC):
                                i, use = c % 2, b * 4 + c // 2
                                dve.wait_ge(s_v[i], FIRST + use + 1)
                                dve.wait_ge(s_acc[i], FIRST + use)
                                nc.vector.tensor_scalar(kt[i][:], psKV[i][:, 0:P], 0.0, WS * EPS, ALU.max,
                                                        ALU.add).then_inc(s_k[i], 1)
                            dve.wait_ge(s_acc[1], FIRST + b * 4 + 4)
                            nc.vector.tensor_copy(kv[:], psA[:, 0:P]).then_inc(s_kvd, 1)
                            nc.vector.tensor_scalar(ksb[:], ones32[:], psA[:, P:P + 1], None, ALU.mult).then_inc(s_kvd, 1)
                            for j in range(2):
                                n = b * 2 + j
                                dve.wait_ge(s_nd, FIRST + n + 1)
                                nc.vector.tensor_scalar(dn[:], psD[:, :], WS * WS * EPS, WS, ALU.add,
                                                        ALU.mult).then_inc(s_dn, 1)
                                dve.wait_ge(s_dn, FIRST + n * 2 + 1)
                                nc.vector.reciprocal(rc[:], dn[:]).then_inc(s_dn, 1)
                                dve.wait_ge(s_dn, FIRST + n * 2 + 2)
                                nc.vector.tensor_tensor(at[j][:], psN[:, :], rc[:], ALU.mult).then_inc(s_at, 1)
                            for j in range(2):
                                cols = ds(b * L + j * ST, ST)
                                dve.wait_ge(s_ot, FIRST + b * 2 + j + 1)
                                nc.vector.tensor_tensor(XT[:, cols], XT[:, cols], ot[j][:], ALU.add).then_inc(s_xu[j], 1)

        def fp4_network():
            CH = 4
            with ExitStack() as tmp:
                sem, stand = scoped(tmp)
                def tb(name, shape, dt=F32):
                    return [tmp.enter_context(nc.sbuf_tensor(f"ff_{name}{j}", shape, dt)) for j in range(2)]
                hs, xq, xqT = tb("hs", [P, ST]), tb("xq", [P, ST]), tb("xqT", [P, ST])
                sg, hh, hq = tb("sg", [P, I_FF]), tb("hh", [P, CH * I_FF]), tb("hq", [P, CH * I_FF])
                hqT, xo, ot = tb("hqT", [P, 3, ST]), tb("xo", [P, ST]), tb("ot", [P, CH, P])
                work = {k: tmp.enter_context(nc.sbuf_tensor("ff_" + k, [P, CH * I_FF], F32)) for k in
                        ("xn", "ab", "q", "r")}
                work |= {k: tmp.enter_context(nc.sbuf_tensor("ff_" + k, [P, CH * I_FF // 16], F32)) for k in
                         ("sc", "rc")}
                s_hs, s_T1, s_xq, s_T2, s_e2, s_T3, s_hq, s_e3, s_Y, s_xo, s_T4, s_e4, s_out, s_mul = (
                    [sem(f"ff_{n}{j}") for j in range(2)] for n in
                    ("hs", "T1", "xq", "T2", "e2", "T3", "hq", "e3", "Y", "xo", "T4", "e4", "out", "mul"))
                s_GU, s_sg, s_m, s_dve = sem("ff_GU"), sem("ff_sg"), sem("ff_m"), sem("ff_dve")
                stand(dma=s_out)
                with nc.Block() as block:
                    @block.tensor
                    def _(pe):
                        with pe.Fori(0, NB) as b:
                            for j in range(2):
                                pe.wait_ge(s_hs[j], FIRST + b + 1)
                                pe.wait_ge(s_e4[j], FIRST + b)
                                for c in range(CH):
                                    t = nc.tensor.transpose(bank[j][:, c * P:(c + 1) * P], hs[j][:, c * P:(c + 1) * P],
                                                            ident[:])
                                t.then_inc(s_T1[j], 1)
                            for j in range(2):
                                pe.wait_ge(s_xq[j], FIRST + b + 1)
                                for c in range(CH):
                                    t = nc.tensor.transpose(bank[j][:, c * P:(c + 1) * P], xq[j][:, c * P:(c + 1) * P],
                                                            ident[:])
                                t.then_inc(s_T2[j], 1)
                                pe.wait_ge(s_e2[j], FIRST + b + 1)
                                for c in range(CH):
                                    n = b * 8 + j * 4 + c
                                    pe.wait_ge(s_m, FIRST + n)
                                    nc.tensor.matmul(bank[2][:, 0:I_FF], xqT[j][:, c * P:(c + 1) * P], wgT[:],
                                                     start=True, stop=True)
                                    nc.tensor.matmul(bank[3][:, 0:I_FF], xqT[j][:, c * P:(c + 1) * P], wuT[:],
                                                     start=True, stop=True).then_inc(s_GU, 1)
                            for j in range(2):
                                pe.wait_ge(s_hq[j], FIRST + b + 1)
                                if j == 1:
                                    pe.wait_ge(s_e3[0], FIRST + b * 3 + 3)
                                for k, n in enumerate(NBLK):
                                    for c in range(CH):
                                        at = c * I_FF + k * P
                                        t = nc.tensor.transpose(bank[4 + k][0:n, c * P:(c + 1) * P],
                                                                hq[j][:, at:at + n], ident[:])
                                    t.then_inc(s_T3[j], 1)
                                pe.wait_ge(s_e3[j], FIRST + b * 3 + 3)
                                if j == 1:
                                    pe.wait_ge(s_xo[0], FIRST + b + 1)
                                for k, n in enumerate(NBLK):
                                    m = nc.tensor.matmul(bank[7][:, :], wdT[0:n, k, :], hqT[j][0:n, k, :],
                                                         start=k == 0, stop=k == 2)
                                m.then_inc(s_Y[j], 1)
                            for j in range(2):
                                pe.wait_ge(s_xo[j], FIRST + b + 1)
                                for c in range(CH):
                                    t = nc.tensor.transpose(bank[j][:, c * P:(c + 1) * P], xo[j][:, c * P:(c + 1) * P],
                                                            ident[:])
                                t.then_inc(s_T4[j], 1)

                    @block.scalar
                    def _(act):
                        with act.Fori(0, NB) as b:
                            for j in range(2):
                                act.wait_ge(s_T1[j], FIRST + b)
                                act.nop(nofuse=True)
                                nc.scalar.copy(hs[j][:], H32[:, ds(b * L + j * ST, ST)]).then_inc(s_hs[j], 1)
                            for j in range(2):
                                act.wait_ge(s_T2[j], FIRST + b + 1)
                                nc.scalar.copy(xqT[j][:], bank[j][:, :]).then_inc(s_e2[j], 1)
                                for c in range(CH):
                                    n = b * 8 + j * 4 + c
                                    act.wait_ge(s_GU, FIRST + n + 1)
                                    nc.scalar.activation(sg[c % 2][:], bank[2][:, 0:I_FF], ACT.Silu).then_inc(s_sg, 1)
                            for j in range(2):
                                for k, n in enumerate(NBLK):
                                    act.wait_ge(s_T3[j], FIRST + b * 3 + k + 1)
                                    nc.scalar.copy(hqT[j][0:n, k, :], bank[4 + k][0:n, :]).then_inc(s_e3[j], 1)
                            for j in range(2):
                                act.wait_ge(s_T4[j], FIRST + b + 1)
                                act.wait_ge(s_out[j], 16 + b * 16)
                                nc.scalar.copy(ot[j][:].rearrange("p c d -> p (c d)"), bank[j][:, :]).then_inc(s_e4[j], 1)

                    @block.vector
                    def _(dve):
                        with dve.Fori(0, NB) as b:
                            step = Chain(dve, s_dve, b, 4 * FP4_STEPS, FIRST)
                            for j in range(2):
                                dve.wait_ge(s_T1[j], FIRST + b + 1)
                                fp4_quant(nc, step, bank[j][:, :], xq[j][:], ST, work).then_inc(s_xq[j], 1)
                                dve.wait_ge(s_xq[j], FIRST + b + 1)
                            for j in range(2):
                                for c in range(CH):
                                    n = b * 8 + j * 4 + c
                                    dve.wait_ge(s_sg, FIRST + n + 1)
                                    nc.vector.tensor_tensor(hh[j][:, c * I_FF:(c + 1) * I_FF], sg[c % 2][:],
                                                            bank[3][:, 0:I_FF], ALU.mult).then_inc(s_m, 1)
                                dve.wait_ge(s_m, FIRST + b * 8 + j * 4 + 4)
                                fp4_quant(nc, step, hh[j][:], hq[j][:], CH * I_FF, work).then_inc(s_hq[j], 1)
                                dve.wait_ge(s_hq[j], FIRST + b + 1)
                            for j in range(2):
                                dve.wait_ge(s_Y[j], FIRST + b + 1)
                                nc.vector.scalar_tensor_tensor(xo[j][:], bank[7][:, :], mod[:, 1, 5, ds(b, 1)],
                                                               XT[:, ds(b * L + j * ST, ST)], ALU.mult,
                                                               ALU.add).then_inc(s_xo[j], 1)
                            step.end()

                    @block.sync
                    def _(sp):
                        with sp.Fori(0, NB) as b:
                            for j in range(2):
                                sp.wait_ge(s_e4[j], FIRST + b + 1)
                                sp.dma_start(out_t[ds(b * 8 + j * 4, 4)].rearrange("c p d -> p c d"),
                                             ot[j][:]).then_inc(s_out[j], 16)
                        for j in range(2):
                            sp.wait_ge(s_out[j], 16 + NB * 16)

        layer_norm("ln0", 0, 0)
        causal_attention()
        layer_norm("ln1", 0, 3)
        router()
        route()
        experts()
        layer_norm("ln2", 1, 0)
        linear_attention()
        H32 = sb("H32", [P, T])
        layer_norm("ln3", 1, 3, H32)
        fp4_network()



_INS = ['L0_attn_x', 'L0_attn_qkv_w', 'L0_attn_qkv_b', 'L0_attn_out_w', 'L0_attn_out_b', 'L0_attn_proj',
        'L0_ffn_Wr', 'L0_ffn_br', 'L0_ffn_Wup', 'L0_ffn_bup', 'L0_ffn_Wgate', 'L0_ffn_bgate', 'L0_ffn_Wdown',
        'L0_ffn_bdown', 'L0_c', 'L0_wmod', 'L1_attn_W_qkv', 'L1_attn_W_out', 'L1_attn_b_out', 'L1_ffn_w_gate',
        'L1_ffn_w_up', 'L1_ffn_w_down', 'L1_c', 'L1_wmod']


_OUTS = [((NB, L, P), 'float32')]


def kernel(**inputs):
    import numpy as _np
    import concourse.bacc as _bacc
    from concourse import mybir as _mybir
    from concourse.bass_utils import run_bass_kernel_spmd as _run

    nc = _bacc.Bacc("TRN2", target_bir_lowering=False, num_devices=1)
    arrays, args = {}, []
    for name in _INS:
        a = _np.ascontiguousarray(inputs[name])
        arrays[f"in_{name}_dram"] = a
        args.append(nc.dram_tensor(f"in_{name}_dram", a.shape, _mybir.dt.from_np(a.dtype), kind="ExternalInput").ap())
    for i, (shape, dtype) in enumerate(_OUTS):
        dt = _mybir.dt.from_np(_np.dtype(dtype))
        args.append(nc.dram_tensor(f"out_{i}_dram", shape, dt, kind="ExternalOutput").ap())
    program(nc, *args)
    r = _run(nc, [arrays], core_ids=[0])
    return r.results[0]["out_0_dram"]
```
